# Optimizing a Trainium2 kernel written in Bass

```python
import numpy as np
import jax
import jax.numpy as jnp

def _softmax(x, axis=-1):
    return jax.nn.softmax(x, axis=axis)

def _gelu(x):
    return jax.nn.gelu(x, approximate=True)

def _silu(x):
    return jax.nn.silu(x)

def _sigmoid(x):
    return jax.nn.sigmoid(x)

def _layernorm(x, axis=-1, eps=1e-05):
    m = jnp.mean(x, axis=axis, keepdims=True)
    v = jnp.var(x, axis=axis, keepdims=True)
    return (x - m) / jnp.sqrt(v + eps)

def _scatter_add(tgt, idx, src, axis=0):
    return tgt.at[idx].add(src)

def _segment_sum(src, seg, n):
    return jax.ops.segment_sum(src, seg, n)
kernel_name = 'mk_perceiver_d1_seqx_r4_9ce5fa'

def setup_inputs(seed: int=0):
    np.random.seed(seed)
    _w = jnp.asarray

    def _rec_inputs():
        import jax
        import jax.numpy as jnp
        _rk = jax.random.key(seed)
        x = -0.0002928 + 1 * jax.random.normal(jax.random.fold_in(_rk, 1), (2, 256, 256), jnp.float32)
        _lenS = 256 - jax.random.randint(jax.random.fold_in(_rk, 7), (2,), 0, max(1, 256 // 4) + 1, jnp.int32)
        _lenS2 = 4096 - jax.random.randint(jax.random.fold_in(_rk, 8), (2,), 0, max(1, 4096 // 4) + 1, jnp.int32)
        _ctx_1024P = jax.random.normal(jax.random.fold_in(_rk, 11), (2, 16, 256), jnp.float32)
        _ctx_1024c = jax.random.dirichlet(jax.random.fold_in(_rk, 511), 0.3 * jnp.ones((16,), jnp.float32), (2, 4096))
        _ctx_1024t = jnp.einsum('bsk,bkd->bsd', _ctx_1024c, _ctx_1024P)
        _ctx_1024t = _ctx_1024t * jax.lax.rsqrt(jnp.mean(jnp.square(_ctx_1024t)) + 1e-12) * 0.953939
        ctx_1024 = -1.39393e-06 + 0.999914 * (_ctx_1024t + 0.3 * jax.random.normal(jax.random.fold_in(_rk, 611), (2, 4096, 256), jnp.float32))
        return (x, ctx_1024)
    x, ctx_1024 = _rec_inputs()

    def _L0_xattn_setup():
        import jax, jax.numpy as jnp
        import numpy as np
        EMB = 256
        DM = 64
        NH = 16
        key = jax.random.key(seed)
        ks = jax.random.split(key, 11)
        bs, slen = (2, 512)
        s = 1.0 / np.sqrt(EMB)
        inp = {'Q': jax.random.normal(ks[0], (bs, slen, EMB), jnp.float32), 'K': jax.random.normal(ks[1], (bs, slen, EMB), jnp.float32), 'V': jax.random.normal(ks[2], (bs, slen, EMB), jnp.float32), 'Wq': jax.random.normal(ks[3], (EMB, DM * NH), jnp.float32) * s, 'bq': jnp.zeros((DM * NH,), jnp.float32), 'Wk': jax.random.normal(ks[4], (EMB, DM * NH), jnp.float32) * s, 'bk': jnp.zeros((DM * NH,), jnp.float32), 'Wv': jax.random.normal(ks[5], (EMB, DM * NH), jnp.float32) * s, 'bv': jnp.zeros((DM * NH,), jnp.float32), 'Wo': jax.random.normal(ks[6], (DM * NH, EMB), jnp.float32) * (1.0 / np.sqrt(DM * NH)), 'bo': jnp.zeros((EMB,), jnp.float32)}
        return inp
    _L0_xattn_all = _L0_xattn_setup()
    _L0_xattn_in = {k: v for k, v in _L0_xattn_all.items() if k in ('Wq', 'bq', 'Wk', 'bk', 'Wv', 'bv', 'Wo', 'bo')}
    del _L0_xattn_all

    def _L0_attn_setup():
        import jax, jax.numpy as jnp
        import numpy as np
        import math
        B, S, D = (4, 512, 256)
        H = 16
        HD = D // H
        DL = 64
        LAMBDA_DECAY = 0.01
        key = jax.random.key(seed)
        ks = jax.random.split(key, 8)
        sc = lambda fan_in: 1.0 / math.sqrt(fan_in)
        return {'x': jax.random.normal(ks[0], (B, S, D), dtype=jnp.float32), 'W_q': jax.random.normal(ks[1], (D, D), dtype=jnp.float32) * sc(D), 'W_k': jax.random.normal(ks[2], (D, D), dtype=jnp.float32) * sc(D), 'W_v': jax.random.normal(ks[3], (D, D), dtype=jnp.float32) * sc(D), 'W_o': jax.random.normal(ks[4], (D, D), dtype=jnp.float32) * sc(D), 'W_down_kv': jax.random.normal(ks[5], (D, DL), dtype=jnp.float32) * sc(D), 'W_up_k': jax.random.normal(ks[6], (DL, D), dtype=jnp.float32) * sc(DL), 'W_up_v': jax.random.normal(ks[7], (DL, D), dtype=jnp.float32) * sc(DL)}
    _L0_attn_all = _L0_attn_setup()
    _L0_attn_in = {k: v for k, v in _L0_attn_all.items() if k in ('W_q', 'W_k', 'W_v', 'W_o', 'W_down_kv', 'W_up_k', 'W_up_v')}
    del _L0_attn_all

    def _L0_ffn_setup():
        import jax, jax.numpy as jnp
        import numpy as np
        BLOCK = 16
        _GRID = jnp.array([0.0, 0.5, 1.0, 1.5, 2.0, 3.0, 4.0, 6.0], dtype=jnp.float32)
        _MID = jnp.array([0.25, 0.75, 1.25, 1.75, 2.5, 3.5, 5.0], dtype=jnp.float32)

        def fp4_quant_dequant(x):
            shape = x.shape
            xb = x.reshape(shape[:-1] + (shape[-1] // BLOCK, BLOCK))
            scale = jnp.max(jnp.abs(xb), axis=-1, keepdims=True) / 6.0
            scale = jnp.maximum(scale, jnp.float32(1e-12))
            xn = xb / scale
            idx = jnp.searchsorted(_MID, jnp.abs(xn))
            q = _GRID[idx] * jnp.sign(xn) * scale
            return q.reshape(shape)

        def fp4_linear(x, w):
            xq = fp4_quant_dequant(x)
            wq = fp4_quant_dequant(w)
            return jnp.einsum('bsk,nk->bsn', xq, wq)
        key = jax.random.key(seed)
        k1, k2, k3, k4 = jax.random.split(key, 4)
        H, I = (256, 704)
        x = jax.random.normal(k1, (4, 1024, H), dtype=jnp.float32)
        w_gate = jax.random.normal(k2, (I, H), dtype=jnp.float32) * 0.02
        w_up = jax.random.normal(k3, (I, H), dtype=jnp.float32) * 0.02
        w_down = jax.random.normal(k4, (H, I), dtype=jnp.float32) * 0.02
        return {'x': x, 'w_gate': w_gate, 'w_up': w_up, 'w_down': w_down}
    _L0_ffn_all = _L0_ffn_setup()
    _L0_ffn_in = {k: v for k, v in _L0_ffn_all.items() if k in ('w_gate', 'w_up', 'w_down')}
    del _L0_ffn_all
    return {'x': x, 'ctx_1024': ctx_1024, 'L0_xattn_Wq': _L0_xattn_in['Wq'], 'L0_xattn_bq': _L0_xattn_in['bq'], 'L0_xattn_Wk': _L0_xattn_in['Wk'], 'L0_xattn_bk': _L0_xattn_in['bk'], 'L0_xattn_Wv': _L0_xattn_in['Wv'], 'L0_xattn_bv': _L0_xattn_in['bv'], 'L0_xattn_Wo': _L0_xattn_in['Wo'], 'L0_xattn_bo': _L0_xattn_in['bo'], 'L0_attn_W_q': _L0_attn_in['W_q'], 'L0_attn_W_k': _L0_attn_in['W_k'], 'L0_attn_W_v': _L0_attn_in['W_v'], 'L0_attn_W_o': _L0_attn_in['W_o'], 'L0_attn_W_down_kv': _L0_attn_in['W_down_kv'], 'L0_attn_W_up_k': _L0_attn_in['W_up_k'], 'L0_attn_W_up_v': _L0_attn_in['W_up_v'], 'L0_ffn_w_gate': _L0_ffn_in['w_gate'], 'L0_ffn_w_up': _L0_ffn_in['w_up'], 'L0_ffn_w_down': _L0_ffn_in['w_down']}

def reference(x, ctx_1024, L0_xattn_Wq, L0_xattn_bq, L0_xattn_Wk, L0_xattn_bk, L0_xattn_Wv, L0_xattn_bv, L0_xattn_Wo, L0_xattn_bo, L0_attn_W_q, L0_attn_W_k, L0_attn_W_v, L0_attn_W_o, L0_attn_W_down_kv, L0_attn_W_up_k, L0_attn_W_up_v, L0_ffn_w_gate, L0_ffn_w_up, L0_ffn_w_down):
    import jax
    import jax.numpy as jnp

    def _L0_xattn_ref(Q, K, V, Wq, bq, Wk, bk, Wv, bv, Wo, bo):
        import jax, jax.numpy as jnp
        import numpy as np
        EMB = 256
        DM = 64
        NH = 16
        bs, q_len, _ = Q.shape
        kv_len = K.shape[1]
        scale = 1.0 / np.sqrt(DM)
        q = (scale * (Q @ Wq + bq)).reshape(bs, q_len, NH, DM)
        k = (K @ Wk + bk).reshape(bs, kv_len, NH, DM)
        v = (V @ Wv + bv).reshape(bs, kv_len, NH, DM)
        qk = jnp.einsum('nlhd,nshd->nhls', q, k)
        a = jax.nn.softmax(qk, axis=-1)
        o = jnp.einsum('nhls,nshd->nlhd', a, v).reshape(bs, q_len, NH * DM)
        return o @ Wo + bo

    def _L0_attn_ref(x, W_q, W_k, W_v, W_o, W_down_kv, W_up_k, W_up_v):
        import jax, jax.numpy as jnp
        import numpy as np
        import math
        B, S, D = (4, 512, 256)
        H = 16
        HD = D // H
        DL = 64
        LAMBDA_DECAY = 0.01
        b, s, d = x.shape
        q = x @ W_q
        k = x @ W_k
        v = x @ W_v
        latent_kv = (k + v) @ W_down_kv
        k_rec = (latent_kv @ W_up_k).reshape(b, s, H, HD).transpose(0, 2, 1, 3)
        v_rec = (latent_kv @ W_up_v).reshape(b, s, H, HD).transpose(0, 2, 1, 3)
        qh = q.reshape(b, s, H, HD).transpose(0, 2, 1, 3)
        scores = jnp.einsum('bhqd,bhkd->bhqk', qh, k_rec) / math.sqrt(d)
        t = jnp.arange(s, dtype=jnp.float32)
        decay = jnp.exp(-LAMBDA_DECAY * jnp.abs(t[:, None] - t[None, :]))
        scores = scores * decay[None, None, :, :]
        attn = jax.nn.softmax(scores, axis=-1)
        out = jnp.einsum('bhqk,bhkd->bhqd', attn, v_rec)
        out = out.transpose(0, 2, 1, 3).reshape(b, s, d)
        return out @ W_o

    def _L0_ffn_ref(x, w_gate, w_up, w_down):
        import jax, jax.numpy as jnp
        import numpy as np
        BLOCK = 16
        _GRID = jnp.array([0.0, 0.5, 1.0, 1.5, 2.0, 3.0, 4.0, 6.0], dtype=jnp.float32)
        _MID = jnp.array([0.25, 0.75, 1.25, 1.75, 2.5, 3.5, 5.0], dtype=jnp.float32)

        def fp4_quant_dequant(x):
            shape = x.shape
            xb = x.reshape(shape[:-1] + (shape[-1] // BLOCK, BLOCK))
            scale = jnp.max(jnp.abs(xb), axis=-1, keepdims=True) / 6.0
            scale = jnp.maximum(scale, jnp.float32(1e-12))
            xn = xb / scale
            idx = jnp.searchsorted(_MID, jnp.abs(xn))
            q = _GRID[idx] * jnp.sign(xn) * scale
            return q.reshape(shape)

        def fp4_linear(x, w):
            xq = fp4_quant_dequant(x)
            wq = fp4_quant_dequant(w)
            return jnp.einsum('bsk,nk->bsn', xq, wq)
        gate = fp4_linear(x, w_gate)
        y = fp4_linear(x, w_up)
        h = jax.nn.silu(gate) * y
        return fp4_linear(h, w_down)
    x = x + _L0_xattn_ref(_layernorm(x, axis=-1), ctx_1024, ctx_1024, L0_xattn_Wq, L0_xattn_bq, L0_xattn_Wk, L0_xattn_bk, L0_xattn_Wv, L0_xattn_bv, L0_xattn_Wo, L0_xattn_bo)
    x = x + _L0_attn_ref(_layernorm(x, axis=-1), L0_attn_W_q, L0_attn_W_k, L0_attn_W_v, L0_attn_W_o, L0_attn_W_down_kv, L0_attn_W_up_k, L0_attn_W_up_v)
    x = x + _L0_ffn_ref(_layernorm(x, axis=-1), L0_ffn_w_gate, L0_ffn_w_up, L0_ffn_w_down)
    return x

_drawn_inputs = setup_inputs


def setup_inputs(seed=0):
    import zlib

    import numpy as np

    out = dict(_drawn_inputs(seed))
    spreads = {'L0_xattn_bq': (0.0, 0.272),
     'L0_xattn_bk': (0.0, 0.8),
     'L0_xattn_bv': (0.0, 0.1),
     'L0_xattn_bo': (0.0, 0.1)}
    factors = {}
    for name, (base, spread) in spreads.items():
        noise = np.random.default_rng([zlib.crc32(name.encode()), seed]).standard_normal(out[name].shape)
        drawn = base * np.exp(spread * noise) if base else spread * noise
        out[name] = jnp.asarray(drawn.astype(out[name].dtype))
    for name, factor in factors.items():
        out[name] = (out[name] * factor).astype(out[name].dtype)
    return out
```

```python
from contextlib import ExitStack

import concourse.bass as bass
from concourse import mybir

ALU = mybir.AluOpType
ACT = mybir.ActivationFunctionType
AX = mybir.AxisListType
F32 = mybir.dt.float32
F32R = mybir.dt.float32r

P = 128


def cross_attention(nc, x, ctx, Wq, bq, Wk, bk, Wv, bv, Wo, ident, y):
    B, S, D = x.shape
    CTX = ctx.shape[1]
    KT = D // P
    HD = 64
    H = Wq.shape[1] // HD
    QT = S // P
    CH = 1024
    NCH = CTX // CH
    PIECE = 512
    NP = CTX // PIECE
    PAIRS = H // 2
    STEPS = 2 * NCH
    GP = B * PAIRS
    N = GP * STEPS
    LEAD = 4
    KPP = PIECE // P
    TB = CH // (2 * P)
    SCALE = float(HD) ** -0.5
    EPS = 1e-5
    assert STEPS == NP and TB * QT == 8

    with ExitStack() as st:
        def ps(name, shape):
            return st.enter_context(nc.psum_tensor(name, shape, F32))

        def tile(name, shape, dt=F32):
            return st.enter_context(nc.sbuf_tensor(name, shape, dt))

        def sem(name):
            return st.enter_context(nc.semaphore(name))

        psS = ps("psS", [P, QT, CH])
        psT = ps("psT", [P, 2, 512])
        psO = ps("psO", [P, 512])
        psW = ps("psW", [P, 512])

        ctxT_hi = tile("ctxT_hi", [P, KT, CTX], F32R)
        ctxT_lo = tile("ctxT_lo", [P, KT, CTX], F32R)
        kT = tile("kT", [P, NP, 2, PIECE], F32R)
        v = tile("v", [P, NP, KPP, 2, 2, HD], F32R)
        kraw = tile("kraw", [P, 2, PIECE])
        vraw = tile("vraw", [P, PIECE])
        prob = tile("prob", [P, QT, CH])
        pT_hi = tile("pT_hi", [P, TB, 512], F32R)
        pT_lo = tile("pT_lo", [P, TB, 512], F32R)
        oT = tile("oT", [P, 2, NCH, S])
        wraw = tile("wraw", [P, 3, KT, P])
        wo = tile("wo", [P, D])
        wk_s = tile("wk_s", [P, 2, KT, P], F32R)
        wv_s = tile("wv_s", [P, 2, KT, P], F32R)
        wq_s = tile("wq_s", [P, 2, KT, 2, 2, HD], F32R)
        qraw = tile("qraw", [P, 2, S])
        q_hi = tile("q_hi", [P, 2, S], F32R)
        q_lo = tile("q_lo", [P, 2, S], F32R)
        xnT_hi = tile("xnT_hi", [P, KT, B * S], F32R)
        xnT_lo = tile("xnT_lo", [P, KT, B * S], F32R)
        cst = tile("cst", [P, KPP, D])
        zeros = tile("zeros", [P, PIECE])
        staging = [cst[:, :, :], oT[:, 0, :, :], oT[:, 1, :, :]]
        prep_banks = [psT[:, 0, :], psT[:, 1, :]] + [psS[:, a, b:b + 512] for a in range(QT) for b in (0, 512)]
        negm = tile("negm", [P, 2, QT, NCH])
        lsum = tile("lsum", [P, 2, QT, NCH])
        negM = tile("negM", [P, 2 * QT])
        dif = tile("dif", [P, 2, QT, NCH])
        edif = tile("edif", [P, 2, QT, NCH])
        le = tile("le", [P, 2, QT, NCH])
        L = tile("L", [P, 2 * QT])
        rL = tile("rL", [P, 2 * QT])
        wts = tile("wts", [P, 2, QT, NCH])
        oweighed = tile("oweighed", [P, NCH, 2 * HD])
        on = tile("on", [P, QT, 2 * HD])
        o2T = tile("o2T", [P, S])
        biases = tile("biases", [P, PAIRS, 4])
        bias = tile("bias", [P, 4])
        bqT = tile("bqT", [P, H])
        bnst = tile("bnst", [P, 6])
        mv = tile("mv", [P, B * QT, 2])
        sd = tile("sd", [P, B * QT])
        epst = tile("epst", [P, 1])
        xn = prob[:, :, :].rearrange("p a (b d) -> p (a b) d", d=D)[:, 0:B * QT, :]

        s_x, s_bias, s_bo = sem("s_x"), sem("s_bias"), sem("s_bo")
        ctx_in = [sem(f"ctx_in{i}") for i in range(3)]
        raw_k, raw_v, raw_q, wo_in = sem("raw_k"), sem("raw_v"), sem("raw_q"), sem("wo_in")
        ident_ok, const_ok = sem("ident_ok"), sem("const_ok")
        ln_step, sd_ok, xn_ok, xnT_ps, xnT_h, xnT_l = (sem(f"ln{i}") for i in range(6))
        bq8_ok, bias_ok = sem("bq8_ok"), sem("bias_ok")
        prep_ps, prep_h, prep_l = sem("prep_ps"), sem("prep_h"), sem("prep_l")
        k_ps, v_ps, kraw_ok, k_split = sem("k_ps"), sem("v_ps"), sem("kraw_ok"), sem("k_split")
        vt_ps, vraw_ok = sem("vt_ps"), sem("vraw_ok")
        v_hi, v_lo = sem("v_hi"), sem("v_lo")
        wk_ok, wv_ok, wq_ok = sem("wk_ok"), sem("wv_ok"), sem("wq_ok")
        q_ps, qraw_ok, q_ok = sem("q_ps"), sem("qraw_ok"), sem("q_ok")
        s_ok, max_ok, exp_ok = sem("s_ok"), sem("max_ok"), sem("exp_ok")
        t_ok, ph_ok, pl_ok, av_ok, oc_ok = (sem(n) for n in ("t_ok", "ph_ok", "pl_ok", "av_ok", "oc_ok"))
        negM_ok, dif_ok, edif_ok, le_ok, L_ok, rL_ok, wts_ok = (
            sem(n) for n in ("negM_ok", "dif_ok", "edif_ok", "le_ok", "L_ok", "rL_ok", "wts_ok"))
        post_ps, comb = sem("post_ps"), sem("comb")
        o2_ps, o2_ok, y_ps, y_ok = sem("o2_ps"), sem("o2_ok"), sem("y_ps"), sem("y_ok")

        def wait(eng, s, val):
            if isinstance(val, int) and val <= 0:
                return
            eng.wait_ge(s, val)

        def column(g):
            return g % PAIRS if isinstance(g, int) else g

        def pairs(eng, body):
            for b in range(B):
                lo = b * PAIRS
                body(lo, 0, b)
                with eng.Fori(lo + 1, lo + PAIRS - 1) as g:
                    body(g, g - lo, b)
                body(lo + PAIRS - 1, PAIRS - 1, b)

        def piece_of(g, c, b, s):
            if s < NP - LEAD:
                return g, c, b, s + LEAD, True
            if isinstance(g, int) and c == PAIRS - 1:
                return g + 1, 0, b + 1, s + LEAD - NP, b + 1 < B
            return g + 1, c + 1, b, s + LEAD - NP, True

        def is_first(g):
            return isinstance(g, int) and g == 0

        def is_last(g):
            return isinstance(g, int) and g == GP - 1

        def preps(g, b):
            return isinstance(g, int) and g % PAIRS == PAIRS - 1 and b + 1 < B

        def prep_at_x1(g, b, s):
            return preps(g, b) and s not in (0, 1, STEPS - 2)

        ctx_t = ctx.rearrange("b (n t p) d -> b n p t d", t=KPP, p=P)

        block = st.enter_context(nc.Block())

        @block.sync
        def _(sp):
            sp.dma_start(y[:, :, :], x.rearrange("b (t p) d -> p (b t) d", p=P)).then_inc(s_x, 16)
            for n in range(3):
                sp.dma_start(staging[n], ctx_t[0, n]).then_inc(ctx_in[n], 16)

            def load_w(g, c):
                for k, (w, s, used) in enumerate(((Wk, raw_k, wk_ok), (Wv, raw_v, wv_ok), (Wq, raw_q, wq_ok))):
                    wait(sp, used, g * (4 if w is Wq else 2))
                    sp.dma_start(wraw[:, k, :, :], w.rearrange("(t p) n -> p t n", p=P)[:, :, bass.ds(c * P, P)])\
                        .then_inc(s, 16)

            load_w(0, 0)
            bias_loads = ((biases[:, :, 0], bk), (biases[:, 1:PAIRS, 1], bv[0:(PAIRS - 1) * P]),
                          (biases[:, 0:1, 1], bv[(PAIRS - 1) * P:PAIRS * P]))
            for dst, src in bias_loads:
                sp.dma_start(dst, src.rearrange("(a p) -> p a", p=P), allow_slow_non_contiguous=True)\
                    .then_inc(s_bias, 16)
            for half in range(2):
                sp.dma_start(bqT[half * HD:(half + 1) * HD, :], bq.rearrange("(h d) -> d h", d=HD), allow_slow_non_contiguous=True)\
                    .then_inc(s_bias, 16)
            for n in range(3, NP):
                sp.wait_ge(prep_ps, KT * (n - 2))
                sp.dma_start(staging[n % 3], ctx_t[0, n]).then_inc(ctx_in[n % 3], 16)

            def body(g, c, b):
                if not is_last(g):
                    ng, nc_, _, _, _ = piece_of(g, c, b, NP - 1)
                    load_w(ng, nc_)
                if preps(g, b):
                    for n in range(NP):
                        sp.wait_ge(prep_ps, 2 * ((b + 1) * NP + n))
                        sp.dma_start(cst[:, :, :], ctx_t[b + 1, n]).then_inc(ctx_in[0], 16)
                wait(sp, y_ps, g)
                sp.dma_start(wo[:, :], Wo[bass.ds(c * P, P), :]).then_inc(wo_in, 16)

            pairs(sp, body)

        @block.gpsimd
        def _(pool):
            pool.memset(zeros[:, :], 0.0).then_inc(const_ok, 1)
            pool.memset(ident[:, :], 0.0).then_inc(const_ok, 1)
            pool.memset(epst[:, :], EPS).then_inc(const_ok, 1)
            pool.wait_ge(const_ok, 3)
            pool.affine_select(out=ident[:, :], in_=ident[:, :], compare_op=ALU.not_equal, fill=1.0, base=0,
                               pattern=[[-1, P]], channel_multiplier=1).then_inc(ident_ok, 1)

            def split_w(g, k, w_s, raw, done):
                wait(pool, raw, 16 * (g + 1))
                src = wraw[:, k, :, :]
                zer = zeros[:, 0:KT * P].rearrange("p (t n) -> p t n", t=KT)
                pool.tensor_tensor(w_s[:, 0, :, :], src, zer, ALU.add).then_inc(done, 1)
                wait(pool, done, 2 * g + 1)
                pool.tensor_tensor(w_s[:, 1, :, :], src, w_s[:, 0, :, :].bitcast(F32), ALU.subtract)\
                    .then_inc(done, 1)
                wait(pool, done, 2 * g + 2)

            def split_wq(g):
                wait(pool, raw_q, 16 * (g + 1))
                src = wraw[:, 2, :, :].rearrange("p t (h d) -> p t h d", h=2)
                zer = zeros[:, 0:KT * P].rearrange("p (t h d) -> p t h d", t=KT, h=2)
                for twin in range(2):
                    pool.tensor_tensor(wq_s[:, 0, :, :, twin, :], src, zer, ALU.add).then_inc(wq_ok, 1)
                wait(pool, wq_ok, 4 * g + 2)
                for twin in range(2):
                    pool.tensor_tensor(wq_s[:, 1, :, :, twin, :], src, wq_s[:, 0, :, :, 0, :].bitcast(F32),
                                       ALU.subtract).then_inc(wq_ok, 1)
                wait(pool, wq_ok, 4 * g + 4)

            def split_piece(m, slot):
                wait(pool, kraw_ok, m + 1)
                raw = kraw[:, slot % 2, :]
                for h in range(2):
                    own = slice(HD * h, HD * h + HD)
                    pool.tensor_tensor(kT[own, slot, h, :], raw[own, :], zeros[own, :], ALU.add)\
                        .then_inc(k_split, 1)
                for h in range(2):
                    wait(pool, k_split, 4 * m + 2 + h)
                    own = slice(HD * h, HD * h + HD)
                    other = slice(HD * (1 - h), HD * (1 - h) + HD)
                    pool.tensor_tensor(kT[other, slot, h, :], raw[own, :], kT[own, slot, h, :].bitcast(F32),
                                       ALU.subtract).then_inc(k_split, 1)
                wait(pool, k_split, 4 * m + 4)

            split_w(0, 0, wk_s, raw_k, wk_ok)
            split_w(0, 1, wv_s, raw_v, wv_ok)
            split_wq(0)
            for m in range(LEAD):
                split_piece(m, m)

            def body(g, c, b):
                for s in range(STEPS):
                    n = g * STEPS + s
                    pg, _, _, slot, some = piece_of(g, c, b, s)
                    if s == NP - LEAD - 1 and not is_last(g):
                        wait(pool, vt_ps, n + LEAD + 1)
                        split_w(g + 1, 1, wv_s, raw_v, wv_ok)
                        wait(pool, k_ps, n + LEAD + 1)
                        split_w(g + 1, 0, wk_s, raw_k, wk_ok)
                    if s == NP - LEAD + 1 and not is_last(g):
                        wait(pool, q_ps, g + 1)
                        split_wq(g + 1)
                    if some:
                        split_piece(n + LEAD, slot)

            pairs(pool, body)

        @block.tensor
        def _(pe):
            mm = pe.matmul

            def scores(n, s, qt, g):
                c, h = s // 2, s % 2
                if qt == 0:
                    if h == 0:
                        wait(pe, k_split, 4 * (n + 2))
                    if s == 0:
                        wait(pe, q_ok, 2 * (g + 1))
                wait(pe, exp_ok, 2 * (n - 1) + qt + 1)
                for i, q in enumerate((q_hi, q_lo)):
                    for half in range(2):
                        last = mm(psS[:, qt, half * PIECE:(half + 1) * PIECE], q[:, h, qt * P:(qt + 1) * P],
                                  kT[:, 2 * c + half, h, :], start=(i == 0), stop=(i == 1))
                last.then_inc(s_ok, 1)

            def turn(n, t):
                if t == 0:
                    wait(pe, exp_ok, 2 * n + 2)
                wait(pe, pl_ok, 4 * n + t - 1)
                for k in range(2):
                    for qt in range(QT):
                        last = pe.transpose(psT[:, t % 2, k * S + qt * P:k * S + qt * P + P],
                                            prob[:, qt, (2 * t + k) * P:(2 * t + k + 1) * P], ident[:, :])
                last.then_inc(t_ok, 1)

            def values(n, s, t):
                c, h = s // 2, s % 2
                wait(pe, pl_ok, 4 * n + t + 1)
                if t == 0:
                    wait(pe, oc_ok, n)
                if h == 0:
                    wait(pe, v_lo, n + t // 2 + 1)
                for k in range(2):
                    kt = 2 * t + k
                    w = v[:, 2 * c + kt // KPP, kt % KPP, h, :, :].rearrange("p a d -> p (a d)")
                    mm(psO[:, 0:S], w, pT_hi[:, t, k * S:(k + 1) * S], start=(kt == 0), stop=False)
                    last = mm(psO[:, 0:S], w, pT_lo[:, t, k * S:(k + 1) * S], start=False,
                              stop=(kt == 2 * TB - 1))
                last.then_inc(av_ok, 1)

            def project(w_s, w_ok, pg, slot, done):
                if slot == 0:
                    wait(pe, w_ok, 2 * pg + 2)
                for i, (a, x_) in enumerate(((0, ctxT_hi), (1, ctxT_hi), (0, ctxT_lo))):
                    for kt in range(KT):
                        last = mm(psW[:, :], w_s[:, a, kt, :], x_[:, kt, slot * PIECE:(slot + 1) * PIECE],
                                  start=(i == 0 and kt == 0), stop=(i == 2 and kt == KT - 1))
                last.then_inc(done, 1)

            def turn_v():
                for k in range(KPP):
                    last = pe.transpose(psW[:, k * P:(k + 1) * P], vraw[:, k * P:(k + 1) * P], ident[:, :])
                last.then_inc(v_ps, 1)

            def project_q(g, b):
                wait(pe, wq_ok, 4 * g + 4)
                for h in range(2):
                    for i, (a, x_) in enumerate(((0, xnT_hi), (1, xnT_hi), (0, xnT_lo))):
                        for kt in range(KT):
                            last = mm(psW[:, h * S:(h + 1) * S],
                                      wq_s[:, a, kt, h, :, :].rearrange("p a d -> p (a d)"),
                                      x_[:, kt, b * S:(b + 1) * S],
                                      start=(i == 0 and kt == 0), stop=(i == 2 and kt == KT - 1))
                last.then_inc(q_ps, 1)

            def turn_ctx(arrived, count, src, kt, dst):
                wait(pe, arrived, count)
                for k in range(KPP):
                    last = pe.transpose(dst[:, k * P:(k + 1) * P], src[:, k, kt * P:(kt + 1) * P], ident[:, :])
                last.then_inc(prep_ps, 1)

            def post(g, h, qt):
                for c in range(NCH):
                    last = pe.transpose(psW[:, c * P:(c + 1) * P], oT[:, h, c, qt * P:(qt + 1) * P], ident[:, :])
                last.then_inc(post_ps, 1)

            def turn_o(g):
                for qt in range(QT):
                    last = pe.transpose(psW[:, qt * P:(qt + 1) * P], on[:, qt, :], ident[:, :])
                last.then_inc(o2_ps, 1)

            def project_o(g):
                wait(pe, wo_in, 16 * (g + 1))
                for qt in range(QT):
                    last = mm(psW[:, qt * D:(qt + 1) * D], o2T[:, qt * P:(qt + 1) * P], wo[:, :],
                              start=True, stop=True)
                last.then_inc(y_ps, 1)

            pe.wait_ge(ident_ok, 1)
            for kt in range(KT):
                pe.wait_ge(xn_ok, B * QT)
                for r in range(B * QT):
                    last = pe.transpose(psS[:, kt, r * P:(r + 1) * P], xn[:, r, kt * P:(kt + 1) * P], ident[:, :])
                last.then_inc(xnT_ps, 1)
            for n in range(NP):
                for kt in range(KT):
                    i = KT * n + kt
                    if i == 2:
                        pe.wait_ge(xnT_l, KT)
                    wait(pe, prep_l, i - len(prep_banks) + 1)
                    turn_ctx(ctx_in[n % 3], 16 * (n // 3 + 1), staging[n % 3], kt, prep_banks[i % len(prep_banks)])
            pe.wait_ge(xnT_l, KT)
            project_q(0, 0)
            for m in range(LEAD):
                wait(pe, prep_l, 2 * m + 2)
                wait(pe, qraw_ok, 2)
                wait(pe, v_lo, m)
                project(wv_s, wv_ok, 0, m, vt_ps)
                pe.wait_ge(vraw_ok, m + 1)
                project(wk_s, wk_ok, 0, m, k_ps)
                pe.wait_ge(kraw_ok, m + 1)
                turn_v()
            pe.wait_ge(prep_l, 2 * NP)
            for qt in range(QT):
                scores(0, 0, qt, 0)

            def body(g, c, b):
                for s in range(STEPS):
                    n = g * STEPS + s
                    pg, _, _, slot, some = piece_of(g, c, b, s)
                    last_step = is_last(g) and s == STEPS - 1
                    if not last_step:
                        for qt in range(QT):
                            scores(n + 1, (s + 1) % STEPS, qt, g + 1 if s == STEPS - 1 else g)
                    turn(n, 0)
                    turn(n, 1)
                    if preps(g, b) and s > 0:
                        wait(pe, prep_l, 2 * ((b + 1) * NP + s))
                    elif b > 0 and isinstance(g, int) and c == 0 and s == 0:
                        wait(pe, prep_l, 2 * (b + 1) * NP)
                    elif s == 1 and not is_first(g):
                        wait(pe, comb, 8 * (g - 1) + 3)
                    elif s == 2 and not is_first(g):
                        wait(pe, comb, 8 * (g - 1) + 7)
                    elif s == 3 and not is_first(g):
                        wait(pe, o2_ok, g)
                    elif s == 4 and not is_first(g):
                        wait(pe, y_ok, g)
                    if some:
                        wait(pe, v_lo, n + LEAD)
                        project(wv_s, wv_ok, pg, slot, vt_ps)
                    turn(n, 2)
                    values(n, s, 0)
                    if some:
                        wait(pe, vraw_ok, n + LEAD + 1)
                        project(wk_s, wk_ok, pg, slot, k_ps)
                    if s in (0, 1) and not is_first(g):
                        wait(pe, oc_ok, (g - 1) * STEPS + 7 + s)
                        wait(pe, kraw_ok, n + LEAD + 1)
                        post(g - 1, s, 0)
                    if s == STEPS - 2 and not is_last(g):
                        wait(pe, kraw_ok, n + LEAD + 1)
                        project_q(g + 1, b + 1 if preps(g, b) else b)
                    if prep_at_x1(g, b, s):
                        wait(pe, kraw_ok, n + LEAD + 1)
                        turn_ctx(ctx_in[0], 16 * (3 + s + 1), cst, 0, psW)
                    turn(n, 3)
                    values(n, s, 1)
                    if some:
                        if s in (0, 1) and not is_first(g):
                            wait(pe, comb, 8 * (g - 1) + 4 * s + 1)
                        elif s == STEPS - 2:
                            wait(pe, qraw_ok, 2 * (g + 2))
                        elif prep_at_x1(g, b, s):
                            wait(pe, prep_l, 2 * ((b + 1) * NP + s) + 1)
                        else:
                            wait(pe, kraw_ok, n + LEAD + 1)
                        turn_v()
                    values(n, s, 2)
                    values(n, s, 3)
                    if s < 4 and not is_first(g):
                        wait(pe, v_lo, n + LEAD + 1)
                    if s in (0, 1) and not is_first(g):
                        post(g - 1, s, 1)
                    elif s == 2 and not is_first(g):
                        wait(pe, comb, 8 * g)
                        turn_o(g - 1)
                    elif s == 3 and not is_first(g):
                        wait(pe, o2_ok, g)
                        project_o(g - 1)
                    if preps(g, b):
                        for kt in range(1 if prep_at_x1(g, b, s) else 0, KT):
                            if kt and not prep_at_x1(g, b, s):
                                wait(pe, prep_l, 2 * ((b + 1) * NP + s) + 1)
                            elif s in (0, 1):
                                wait(pe, comb, 8 * (g - 1) + 4 * s + 3)
                            elif s == 2:
                                wait(pe, o2_ok, g)
                            elif s == 3:
                                wait(pe, y_ok, g)
                            else:
                                wait(pe, v_lo, n + LEAD + 1)
                            turn_ctx(ctx_in[0], 16 * (3 + s + 1), cst, kt, psW)

            pairs(pe, body)
            wait(pe, oc_ok, N)
            wait(pe, y_ok, GP - 1)
            wait(pe, v_lo, N)
            for k, (h, qt) in enumerate(((0, 0), (0, 1), (1, 0), (1, 1))):
                wait(pe, comb, 8 * (GP - 1) + 2 * k - 1 if k else 0)
                post(GP - 1, h, qt)
            pe.wait_ge(comb, 8 * GP)
            turn_o(GP - 1)
            pe.wait_ge(o2_ok, GP)
            project_o(GP - 1)

        @block.scalar
        def _(act):
            def split_hi(dst, src, done):
                act.activation(dst, src, ACT.Copy).then_inc(done, 1)

            def exp(n, s, qt, g):
                c, h = s // 2, s % 2
                wait(act, max_ok, 2 * n + qt + 1)
                if qt == 0:
                    wait(act, t_ok, 4 * n)
                if s == 0 and qt == 0:
                    wait(act, le_ok, g)
                act.activation(prob[:, qt, :], psS[:, qt, :], ACT.Exp, bias=negm[:, h, qt, c:c + 1],
                               accum_out=lsum[:, h, qt, c:c + 1]).then_inc(exp_ok, 1)

            def raw_k_(m, pg, slot):
                if slot == 0:
                    wait(act, bias_ok, pg + 1)
                wait(act, k_ps, m + 1)
                wait(act, k_split, 4 * (m - 1))
                act.activation(kraw[:, slot % 2, :], psW[:, :], ACT.Identity, bias=bias[:, 0:1])\
                   .then_inc(kraw_ok, 1)

            def v_raw(m):
                wait(act, vt_ps, m + 1)
                act.activation(vraw[:, :], psW[:, :], ACT.Copy).then_inc(vraw_ok, 1)

            def v_hi_(m, slot):
                wait(act, v_ps, m + 1)
                split_hi(v[:, slot, :, :, 0, :], psW[:, :].rearrange("p (k h d) -> p k h d", k=KPP, h=2), v_hi)

            def q_raw(g):
                wait(act, bias_ok, g + 1)
                wait(act, q_ps, g + 1)
                for h in range(2):
                    act.activation(qraw[:, h, :], psW[:, h * S:(h + 1) * S], ACT.Identity, scale=SCALE,
                                   bias=bias[:, 2 + h:3 + h]).then_inc(qraw_ok, 1)

            def prep_hi(count, kt, piece, src):
                wait(act, prep_ps, 2 * count + kt + 1)
                split_hi(ctxT_hi[:, kt, piece * PIECE:(piece + 1) * PIECE], src, prep_h)

            def p_hi(n, t):
                wait(act, t_ok, 4 * n + t + 1)
                wait(act, av_ok, 4 * n + t - TB + 1)
                split_hi(pT_hi[:, t, :], psT[:, t % 2, :], ph_ok)

            def o2(g):
                wait(act, o2_ps, g + 1)
                act.activation(o2T[:, :], psW[:, 0:S], ACT.Identity, bias=bias[:, 1:2])\
                   .then_inc(o2_ok, 1)

            act.wait_ge(ln_step, 2 * B * QT)
            act.wait_ge(const_ok, 3)
            act.activation(sd[:, :], mv[:, :, 1], ACT.Sqrt, bias=epst[:, 0:1]).then_inc(sd_ok, 1)
            for kt in range(KT):
                act.wait_ge(xnT_ps, kt + 1)
                split_hi(xnT_hi[:, kt, :], psS[:, kt, 0:B * S], xnT_h)
            for n in range(NP):
                for kt in range(KT):
                    prep_hi(n, kt, n, prep_banks[(KT * n + kt) % len(prep_banks)])
            q_raw(0)
            for m in range(LEAD):
                v_raw(m)
                raw_k_(m, 0, m)
                v_hi_(m, m)
            for qt in range(QT):
                exp(0, 0, qt, 0)

            def body(g, c, b):
                for s in range(STEPS):
                    n = g * STEPS + s
                    pg, _, _, slot, some = piece_of(g, c, b, s)
                    if s == STEPS - 1:
                        wait(act, dif_ok, g + 1)
                        act.activation(edif[:, :, :, :], dif[:, :, :, :], ACT.Exp).then_inc(edif_ok, 1)
                    p_hi(n, 0)
                    p_hi(n, 1)
                    if some:
                        v_raw(n + LEAD)
                    p_hi(n, 2)
                    if some:
                        raw_k_(n + LEAD, pg, slot)
                    if s == STEPS - 2 and not is_last(g):
                        q_raw(g + 1)
                    if prep_at_x1(g, b, s):
                        prep_hi((b + 1) * NP + s, 0, s, psW[:, :])
                    p_hi(n, 3)
                    if some:
                        v_hi_(n + LEAD, slot)
                    if not (is_last(g) and s == STEPS - 1):
                        for qt in range(QT):
                            exp(n + 1, (s + 1) % STEPS, qt, g + 1 if s == STEPS - 1 else g)
                    wait(act, av_ok, 4 * n + 4)
                    if s == 0:
                        wait(act, post_ps, 4 * g - 2)
                    if s == 1:
                        wait(act, post_ps, 4 * g)
                    act.activation(oT[:, s % 2, s // 2, :], psO[:, 0:S], ACT.Copy).then_inc(oc_ok, 1)
                    if s == 2 and not is_first(g):
                        o2(g - 1)
                    if preps(g, b):
                        for kt in range(1 if prep_at_x1(g, b, s) else 0, KT):
                            prep_hi((b + 1) * NP + s, kt, s, psW[:, :])

            pairs(act, body)
            o2(GP - 1)

        @block.vector
        def _(dve):
            def maximum(n, s, qt, g):
                c, h = s // 2, s % 2
                wait(dve, s_ok, 2 * n + qt + 1)
                dve.tensor_reduce(negm[:, h, qt, c:c + 1], psS[:, qt, :], AX.X, ALU.max, negate=True)\
                   .then_inc(max_ok, 1)

            def p_lo(n, t):
                wait(dve, ph_ok, 4 * n + t + 1)
                dve.tensor_tensor(pT_lo[:, t, :], psT[:, t % 2, :], pT_hi[:, t, :].bitcast(F32), ALU.subtract)\
                   .then_inc(pl_ok, 1)

            def v_lo_(m, slot):
                wait(dve, v_hi, m + 1)
                dve.tensor_tensor(v[:, slot, :, :, 1, :], psW[:, :].rearrange("p (k h d) -> p k h d", k=KPP, h=2),
                                  v[:, slot, :, :, 0, :].bitcast(F32), ALU.subtract).then_inc(v_lo, 1)

            def split_q(g):
                wait(dve, qraw_ok, 2 * g + 2)
                wait(dve, s_ok, 2 * STEPS * g)
                dve.tensor_copy(q_hi[:, :, :], qraw[:, :, :]).then_inc(q_ok, 1)
                wait(dve, q_ok, 2 * g + 1)
                dve.tensor_tensor(q_lo[:, :, :], qraw[:, :, :], q_hi[:, :, :].bitcast(F32), ALU.subtract)\
                   .then_inc(q_ok, 1)

            def prep_lo(count, kt, piece, src):
                wait(dve, prep_h, 2 * count + kt + 1)
                keys = slice(piece * PIECE, (piece + 1) * PIECE)
                dve.tensor_tensor(ctxT_lo[:, kt, keys], src, ctxT_hi[:, kt, keys].bitcast(F32), ALU.subtract)\
                   .then_inc(prep_l, 1)

            def weigh(g):
                v4 = lambda a: a[:, :, :, :].rearrange("p h q c -> p (h q) c")
                wide = lambda a: a[:, :].unsqueeze(2).to_broadcast([P, 2 * QT, NCH])
                wait(dve, max_ok, 2 * STEPS * (g + 1))
                dve.tensor_reduce(negM[:, :], v4(negm), AX.X, ALU.min).then_inc(negM_ok, 1)
                wait(dve, negM_ok, g + 1)
                dve.tensor_tensor(v4(dif), wide(negM), v4(negm), ALU.subtract).then_inc(dif_ok, 1)

            def weigh_end(g):
                v4 = lambda a: a[:, :, :, :].rearrange("p h q c -> p (h q) c")
                wide = lambda a: a[:, :].unsqueeze(2).to_broadcast([P, 2 * QT, NCH])
                wait(dve, edif_ok, g + 1)
                wait(dve, exp_ok, 2 * STEPS * (g + 1))
                dve.tensor_tensor(v4(le), v4(edif), v4(lsum), ALU.mult).then_inc(le_ok, 1)
                wait(dve, le_ok, g + 1)
                dve.tensor_reduce(L[:, :], v4(le), AX.X, ALU.add).then_inc(L_ok, 1)
                wait(dve, L_ok, g + 1)
                dve.reciprocal(rL[:, :], L[:, :]).then_inc(rL_ok, 1)
                wait(dve, rL_ok, g + 1)
                dve.tensor_tensor(v4(wts), v4(edif), wide(rL), ALU.mult).then_inc(wts_ok, 1)

            def combine(g, k):
                h, qt = k // QT, k % QT
                base = 8 * g + 2 * k
                wait(dve, post_ps, 4 * g + k + 1)
                if k == 0:
                    wait(dve, wts_ok, g + 1)
                    wait(dve, o2_ps, g)
                wait(dve, comb, base)
                dve.tensor_tensor(oweighed[:, :, :], psW[:, :].rearrange("p (c d) -> p c d", c=NCH),
                                  wts[:, h, qt, :].unsqueeze(2).to_broadcast([P, NCH, 2 * HD]), ALU.mult)\
                   .then_inc(comb, 1)
                wait(dve, comb, base + 1)
                dve.tensor_reduce(on[:, qt, h * HD:(h + 1) * HD],
                                  oweighed[:, :, :].rearrange("p c (a d) -> p d (c a)", a=2), AX.X, ALU.add)\
                   .then_inc(comb, 1)

            def add_y(g, b):
                wait(dve, y_ps, g + 1)
                wait(dve, y_ok, g)
                rows = y[:, b * QT:(b + 1) * QT, :].rearrange("p q d -> p (q d)")
                dve.tensor_tensor(rows, psW[:, :], rows, ALU.add).then_inc(y_ok, 1)

            def take_bias(g, c):
                wait(dve, kraw_ok, STEPS * g)
                wait(dve, o2_ok, g - 1)
                dve.tensor_scalar(bias[:, :].unsqueeze(1), biases[:, bass.ds(c, 1), :], 1.0, None, ALU.mult)\
                   .then_inc(bias_ok, 1)

            dve.wait_ge(s_x, 16)
            for r in range(B * QT):
                wait(dve, ln_step, 2 * r)
                dve.bn_stats(bnst[:, :], y[:, r, :]).then_inc(ln_step, 1)
                wait(dve, ln_step, 2 * r + 1)
                dve.bn_aggr(mv[:, r, :], bnst[:, :]).then_inc(ln_step, 1)
            dve.wait_ge(sd_ok, 1)
            dve.reciprocal(sd[:, :], sd[:, :]).then_inc(sd_ok, 1)
            dve.wait_ge(sd_ok, 2)
            for r in range(B * QT):
                dve.tensor_scalar(xn[:, r, :], y[:, r, :], mv[:, r, 0:1], sd[:, r:r + 1], ALU.subtract, ALU.mult)\
                   .then_inc(xn_ok, 1)
            for kt in range(KT):
                dve.wait_ge(xnT_h, kt + 1)
                dve.tensor_tensor(xnT_lo[:, kt, :], psS[:, kt, 0:B * S], xnT_hi[:, kt, :].bitcast(F32),
                                  ALU.subtract).then_inc(xnT_l, 1)
            dve.wait_ge(s_bias, 16 * 5)
            dve.tensor_scalar(biases[:, :, 2:4], bqT[:, :].rearrange("p (a h) -> p a h", h=2), SCALE, None,
                              ALU.mult).then_inc(bq8_ok, 1)
            dve.wait_ge(bq8_ok, 1)
            take_bias(0, 0)
            for n in range(NP):
                for kt in range(KT):
                    prep_lo(n, kt, n, prep_banks[(KT * n + kt) % len(prep_banks)])
            split_q(0)
            for m in range(LEAD):
                v_lo_(m, m)
            for qt in range(QT):
                maximum(0, 0, qt, 0)

            def body(g, c, b):
                for s in range(STEPS):
                    n = g * STEPS + s
                    _, _, _, slot, some = piece_of(g, c, b, s)
                    more = not (is_last(g) and s == STEPS - 1)
                    if s == STEPS - 1:
                        weigh(g)
                    if more:
                        if s == STEPS - 1:
                            wait(dve, dif_ok, g + 1)
                        maximum(n + 1, (s + 1) % STEPS, 0, g)
                    if s == STEPS - 1:
                        weigh_end(g)
                    p_lo(n, 0)
                    p_lo(n, 1)
                    if more:
                        maximum(n + 1, (s + 1) % STEPS, 1, g)
                    p_lo(n, 2)
                    if s in (0, 1) and not is_first(g):
                        combine(g - 1, 2 * s)
                    if s == STEPS - 2 and not is_last(g):
                        split_q(g + 1)
                    if prep_at_x1(g, b, s):
                        prep_lo((b + 1) * NP + s, 0, s, psW[:, :])
                    p_lo(n, 3)
                    if some:
                        v_lo_(n + LEAD, slot)
                    if s in (0, 1) and not is_first(g):
                        combine(g - 1, 2 * s + 1)
                    if s == 3 and not is_first(g):
                        add_y(g - 1, b - 1 if isinstance(g, int) and c == 0 else b)
                    if s == NP - LEAD - 1:
                        take_bias(g + 1, piece_of(g, c, b, NP - 1)[1])
                    if preps(g, b):
                        for kt in range(1 if prep_at_x1(g, b, s) else 0, KT):
                            prep_lo((b + 1) * NP + s, kt, s, psW[:, :])

            pairs(dve, body)
            for k in range(2 * QT):
                combine(GP - 1, k)
            add_y(GP - 1, B - 1)


def self_attention(nc, W_q, W_k, W_v, W_o, W_down_kv, W_up_k, W_up_v, bo, ident, y):
    D = W_q.shape[0]
    KT = D // P
    R = y.shape[1]
    QT = 2
    B = R // QT
    S = QT * P
    H = 16
    HD = D // H
    HPT = P // HD
    DL = W_down_kv.shape[1]
    DECAY = 0.01
    EPS = 1e-5
    U = B * H

    with ExitStack() as st:
        def ps(name, shape):
            return st.enter_context(nc.psum_tensor(name, shape, F32))

        def tile(name, shape, dt=F32):
            return st.enter_context(nc.sbuf_tensor(name, shape, dt))

        def sem(name):
            return st.enter_context(nc.semaphore(name))

        psP = ps("saP", [P, 2, 512])
        psS = ps("saS", [P, 2, QT, S])
        psT = ps("saT", [P, 2, KT, S])
        psO = ps("saO", [P, B, QT, D])

        w = tile("sa_w", [P, 4, KT, D])
        wd = tile("sa_wd", [P, KT, DL])
        wu = tile("sa_wu", [DL, 2, D])
        bot = tile("sa_bo", [P, D])
        xn = tile("sa_xn", [P, R, D])
        xnT = tile("sa_xnT", [P, KT, R * P])
        kvT = tile("sa_kvT", [P, KT, R * P])
        latT = tile("sa_latT", [DL, R * P])
        kT = tile("sa_kT", [P, KT, R * P])
        vr = tile("sa_v", [P, R, D])
        qT = tile("sa_qT", [P, KT, R * P])
        qm = tile("sa_qm", [P, H, R * P])
        hm = tile("sa_hm", [P, HPT])
        rel = tile("sa_rel", [P, QT, S])
        relf = tile("sa_relf", [P, QT, S])
        decay = tile("sa_decay", [P, QT, S])
        sd_ = tile("sa_s", [P, 2, QT, S])
        negm = tile("sa_negm", [P, U, QT])
        lsum = tile("sa_l", [P, B, QT, H])
        rl = tile("sa_rl", [P, B, QT, H])
        pr = tile("sa_p", [P, 2, QT, S])
        pT = tile("sa_pT", [P, 2, KT, S])
        o = tile("sa_o", [P, R, D])
        oT = tile("sa_oT", [P, KT, R * P])
        bnst = tile("sa_bn", [P, 6])
        mv = tile("sa_mv", [P, R, 2])
        sd = tile("sa_sd", [P, R])
        epst = tile("sa_eps", [P, 1])

        w_in = [sem(f"sa_w{i}") for i in range(7)]
        bo_in = sem("sa_bo_in")
        const, masks = sem("sa_const"), sem("sa_masks")
        x1_ok, stat_ok, sd_ok, xn_ok = sem("sa_x1"), sem("sa_stat"), sem("sa_sdok"), sem("sa_xnok")
        decay_a, decay_ok = sem("sa_decay_a"), sem("sa_decay_ok")
        proj_ps, proj_ok = sem("sa_proj_ps"), sem("sa_proj_ok")
        qm_ok = sem("sa_qm_ok")
        s_ok, sd_done, max_ok, exp_ok = sem("sa_s_ok"), sem("sa_sd"), sem("sa_max"), sem("sa_exp")
        t_ok, pT_ok, av_ok = sem("sa_t"), sem("sa_pTok"), sem("sa_av")
        rl_ok, on_ok, out_ps, out_ok = sem("sa_rlok"), sem("sa_on"), sem("sa_out_ps"), sem("sa_out")

        plan = [("x", 0), ("x", 1), ("kv", 0), ("kv", 1), ("q", 0), ("q", 1), ("lat", 0),
                ("k", 0), ("k", 1), ("v", 0), ("v", 1)]
        at = {key: n for n, key in enumerate(plan)}

        block = st.enter_context(nc.Block())

        @block.sync
        def _(sp):
            sp.dma_start(bot[:, :], bo.rearrange("(o n) -> o n", o=1).to_broadcast([P, D])).then_inc(bo_in, 16)
            for i, a in enumerate((W_k, W_v, W_q)):
                sp.dma_start(w[:, i, :, :], a.rearrange("(t p) n -> p t n", p=P)).then_inc(w_in[i], 16)
            sp.dma_start(wd[:, :, :], W_down_kv.rearrange("(t p) n -> p t n", p=P)).then_inc(w_in[4], 16)
            sp.dma_start(wu[:, 0, :], W_up_k).then_inc(w_in[5], 16)
            sp.dma_start(wu[:, 1, :], W_up_v).then_inc(w_in[6], 16)
            sp.dma_start(w[:, 3, :, :], W_o.rearrange("(t p) n -> p t n", p=P)).then_inc(w_in[3], 16)

        @block.gpsimd
        def _(pool):
            pool.memset(epst[:, :], EPS).then_inc(const, 1)
            pool.memset(hm[:, :], 1.0).then_inc(const, 1)
            pool.iota(rel[:, :, :], [[P, QT], [-1, S]], base=0, channel_multiplier=1,
                      allow_small_or_imprecise_dtypes=True).then_inc(const, 1)
            pool.wait_ge(const, 3)
            pool.affine_select(out=hm[:, :], in_=hm[:, :], compare_op=ALU.is_ge, fill=0.0, base=0,
                               pattern=[[-HD, HPT]], channel_multiplier=1).then_inc(masks, 1)
            pool.wait_ge(masks, 1)
            pool.affine_select(out=hm[:, :], in_=hm[:, :], compare_op=ALU.is_ge, fill=0.0, base=HD - 1,
                               pattern=[[HD, HPT]], channel_multiplier=-1).then_inc(masks, 1)

        @block.tensor
        def _(pe):
            mm = pe.matmul

            def step(key, emit):
                n = at[key]
                if n >= 2:
                    pe.wait_ge(proj_ok, n - 1)
                emit(psP[:, n % 2, :]).then_inc(proj_ps, 1)

            def turn_x(kt):
                def emit(dst):
                    for r in range(R):
                        last = pe.transpose(dst[:, r * P:(r + 1) * P], xn[:, r, kt * P:(kt + 1) * P], ident[:, :])
                    return last
                return emit

            def product(pairs):
                def emit(dst):
                    for i, (a, b) in enumerate(pairs):
                        last = mm(dst[0:a.shape[1], 0:b.shape[1]], a, b, start=(i == 0),
                                  stop=(i == len(pairs) - 1))
                    return last
                return emit

            def rows_of_v(half):
                def emit(dst):
                    for j in range(2):
                        r = 2 * half + j
                        last = mm(dst[:, j * D:(j + 1) * D], latT[:, r * P:(r + 1) * P], wu[:, 1, :],
                                  start=True, stop=True)
                    return last
                return emit

            cols = lambda d: slice(d * P, (d + 1) * P)
            pe.wait_ge(xn_ok, R)
            for kt in range(KT):
                step(("x", kt), turn_x(kt))
            pe.wait_ge(proj_ok, at[("x", 1)] + 1)
            pe.wait_ge(w_in[0], 16)
            pe.wait_ge(w_in[1], 16)
            for d in range(KT):
                step(("kv", d), product([(w[:, i, kt, cols(d)], xnT[:, kt, :]) for i in range(2) for kt in range(KT)]))
            pe.wait_ge(w_in[2], 16)
            for d in range(KT):
                step(("q", d), product([(w[:, 2, kt, cols(d)], xnT[:, kt, :]) for kt in range(KT)]))
            pe.wait_ge(w_in[4], 16)
            pe.wait_ge(proj_ok, at[("kv", 1)] + 1)
            step(("lat", 0), product([(wd[:, kt, :], kvT[:, kt, :]) for kt in range(KT)]))
            pe.wait_ge(w_in[5], 16)
            pe.wait_ge(w_in[6], 16)
            pe.wait_ge(proj_ok, at[("lat", 0)] + 1)
            for d in range(KT):
                step(("k", d), product([(wu[:, 0, cols(d)], latT[:, :])]))
            for half in range(2):
                step(("v", half), rows_of_v(half))

            def scores(u):
                b, h = u // H, u % H
                if u == 0:
                    pe.wait_ge(proj_ok, at[("k", 1)] + 1)
                if b == 0:
                    pe.wait_ge(qm_ok, h + 1)
                if u >= 2:
                    pe.wait_ge(sd_done, u - 1)
                for qt in range(QT):
                    r = b * QT + qt
                    last = mm(psS[:, u % 2, qt, :], qm[:, h, r * P:(r + 1) * P],
                              kT[:, h // HPT, b * S:(b + 1) * S], start=True, stop=True)
                last.then_inc(s_ok, 1)

            def turn(u):
                pe.wait_ge(exp_ok, 2 * (u + 1))
                if u >= 2:
                    pe.wait_ge(pT_ok, u - 1)
                for kt in range(KT):
                    for qt in range(QT):
                        last = pe.transpose(psT[:, u % 2, kt, qt * P:(qt + 1) * P],
                                            pr[:, u % 2, qt, kt * P:(kt + 1) * P], ident[:, :])
                last.then_inc(t_ok, 1)

            def values(u):
                b, h = u // H, u % H
                if u == 0:
                    pe.wait_ge(proj_ok, len(plan))
                pe.wait_ge(pT_ok, u + 1)
                for qt in range(QT):
                    for kt in range(KT):
                        last = mm(psO[:, b, qt, h * HD:(h + 1) * HD], pT[:, u % 2, kt, qt * P:(qt + 1) * P],
                                  vr[:, b * KT + kt, h * HD:(h + 1) * HD], start=(kt == 0), stop=(kt == KT - 1))
                last.then_inc(av_ok, 1)

            for i in range(U + 3):
                if i < U:
                    scores(i)
                if 2 <= i < U + 2:
                    turn(i - 2)
                if i >= 3:
                    values(i - 3)
            pe.wait_ge(w_in[3], 16)
            for kt in range(KT):
                pe.wait_ge(on_ok, R)
                for r in range(R):
                    last = pe.transpose(psP[:, kt, r * P:(r + 1) * P], o[:, r, kt * P:(kt + 1) * P], ident[:, :])
                last.then_inc(out_ps, 1)
            pe.wait_ge(out_ok, KT)
            for half in range(2):
                for j in range(2):
                    r = 2 * half + j
                    for kt in range(KT):
                        last = mm(psS[:, half, j, :], oT[:, kt, r * P:(r + 1) * P], w[:, 3, kt, :],
                                  start=(kt == 0), stop=(kt == KT - 1))
                last.then_inc(out_ps, 1)

        @block.scalar
        def _(act):
            act.wait_ge(stat_ok, 2 * R)
            act.wait_ge(const, 1)
            act.activation(sd[:, :], mv[:, :, 1], ACT.Sqrt, bias=epst[:, 0:1]).then_inc(sd_ok, 1)
            act.wait_ge(const, 3)
            act.activation(relf[:, :, :], rel[:, :, :], ACT.Abs).then_inc(decay_a, 1)
            act.wait_ge(decay_a, 1)
            act.activation(rel[:, :, :], relf[:, :, :], ACT.Exp, scale=-DECAY).then_inc(decay_a, 1)

            def copy_out(key, dst, width=512, rows=P):
                n = at[key]
                act.wait_ge(proj_ps, n + 1)
                act.activation(dst, psP[0:rows, n % 2, 0:width], ACT.Copy).then_inc(proj_ok, 1)

            for kt in range(KT):
                copy_out(("x", kt), xnT[:, kt, :])
            for d in range(KT):
                copy_out(("kv", d), kvT[:, d, :])
            for d in range(KT):
                copy_out(("q", d), qT[:, d, :])
            copy_out(("lat", 0), latT[:, :], rows=DL)
            for d in range(KT):
                copy_out(("k", d), kT[:, d, :])
            for half in range(2):
                copy_out(("v", half), vr[:, 2 * half:2 * half + 2, :].rearrange("p a d -> p (a d)"))
            for u in range(U + 2):
                if u < U:
                    b, h = u // H, u % H
                    act.wait_ge(max_ok, u + 1)
                    if u >= 2:
                        act.wait_ge(t_ok, u - 1)
                    for qt in range(QT):
                        act.activation(pr[:, u % 2, qt, :], sd_[:, u % 2, qt, :], ACT.Exp,
                                       bias=negm[:, u, qt:qt + 1], accum_out=lsum[:, b, qt, h:h + 1])\
                           .then_inc(exp_ok, 1)
                if u >= 2:
                    n = u - 2
                    act.wait_ge(t_ok, n + 1)
                    if n >= 2:
                        act.wait_ge(av_ok, n - 1)
                    act.activation(pT[:, n % 2, :, :], psT[:, n % 2, :, :], ACT.Copy).then_inc(pT_ok, 1)
            for kt in range(KT):
                act.wait_ge(out_ps, kt + 1)
                act.activation(oT[:, kt, :], psP[:, kt, :], ACT.Copy).then_inc(out_ok, 1)

        @block.vector
        def _(dve):
            dve.wait_ge(bo_in, 16)
            for r in range(R):
                dve.tensor_tensor(y[:, r, :], y[:, r, :], bot[:, :], ALU.add).then_inc(x1_ok, 1)
            for r in range(R):
                dve.wait_ge(x1_ok, r + 1)
                if r:
                    dve.wait_ge(stat_ok, 2 * r)
                dve.bn_stats(bnst[:, :], y[:, r, :]).then_inc(stat_ok, 1)
                dve.wait_ge(stat_ok, 2 * r + 1)
                dve.bn_aggr(mv[:, r, :], bnst[:, :]).then_inc(stat_ok, 1)
            dve.wait_ge(sd_ok, 1)
            dve.reciprocal(sd[:, :], sd[:, :]).then_inc(sd_ok, 1)
            dve.wait_ge(sd_ok, 2)
            for r in range(R):
                dve.tensor_scalar(xn[:, r, :], y[:, r, :], mv[:, r, 0:1], sd[:, r:r + 1], ALU.subtract, ALU.mult)\
                   .then_inc(xn_ok, 1)
            dve.wait_ge(decay_a, 2)
            dve.tensor_scalar(decay[:, :, :], rel[:, :, :], float(D) ** -0.5, None, ALU.mult).then_inc(decay_ok, 1)
            dve.wait_ge(masks, 2)
            for h in range(H):
                dve.wait_ge(proj_ok, at[("q", h // HPT)] + 1)
                dve.tensor_scalar(qm[:, h, :], qT[:, h // HPT, :], hm[:, h % HPT:h % HPT + 1], None, ALU.mult)\
                   .then_inc(qm_ok, 1)
            dve.wait_ge(decay_ok, 1)
            for u in range(U):
                dve.wait_ge(s_ok, u + 1)
                if u >= 2:
                    dve.wait_ge(exp_ok, 2 * (u - 1))
                dve.tensor_tensor(sd_[:, u % 2, :, :], psS[:, u % 2, :, :], decay[:, :, :], ALU.mult)\
                   .then_inc(sd_done, 1)
                dve.wait_ge(sd_done, u + 1)
                dve.tensor_reduce(negm[:, u, :], sd_[:, u % 2, :, :], AX.X, ALU.max, negate=True)\
                   .then_inc(max_ok, 1)
            dve.wait_ge(exp_ok, 2 * U)
            dve.reciprocal(rl[:, :, :, :], lsum[:, :, :, :]).then_inc(rl_ok, 1)
            dve.wait_ge(rl_ok, 1)
            dve.wait_ge(av_ok, U)
            for r in range(R):
                b, qt = r // QT, r % QT
                heads = lambda a: a.rearrange("p (h d) -> p h d", h=H)
                dve.tensor_tensor(heads(o[:, r, :]), heads(psO[:, b, qt, :]),
                                  rl[:, b, qt, :].unsqueeze(2).to_broadcast([P, H, HD]), ALU.mult)\
                   .then_inc(on_ok, 1)
            for half in range(2):
                dve.wait_ge(out_ps, KT + half + 1)
                rows = y[:, 2 * half:2 * half + 2, :]
                dve.tensor_tensor(rows, psS[:, half, :, :], rows, ALU.add).then_inc(x1_ok, 1)


def fp4_ffn(nc, w_gate, w_up, w_down, ident, y, out):
    F, D = w_gate.shape
    KT = D // P
    R = y.shape[1]
    BLOCK = 16
    FT = (F + P - 1) // P
    EPS = 1e-5
    rows_of = lambda j: min(P, F - j * P)

    with ExitStack() as st:
        def ps(name, shape):
            return st.enter_context(nc.psum_tensor(name, shape, F32))

        def tile(name, shape, dt=F32):
            return st.enter_context(nc.sbuf_tensor(name, shape, dt))

        def sem(name):
            return st.enter_context(nc.semaphore(name))

        psG = ps("ffG", [P, 1024])
        psU = ps("ffU", [P, 1024])
        psX = ps("ffX", [P, 2, 512])
        psD = ps("ffD", [P, 2, 512])

        WB = 2 * FT * D
        win = tile("ff_win", [P, 2, FT, D])
        wdn = tile("ff_wdn", [P, KT, F])
        wgT = tile("ff_wgT", [P, 2, KT, F])
        wdT = tile("ff_wdT", [P, FT, D])
        xn = tile("ff_xn", [P, R, D])
        xqT = tile("ff_xqT", [P, KT, R * P])
        eg = tile("ff_eg", [P, 2, F])
        hh = tile("ff_h", [P, 2, F])
        hT = tile("ff_hT", [P, 2, FT, P])
        res = tile("ff_res", [P, R, D])
        absx = tile("ff_abs", [P, WB])
        cnt = tile("ff_cnt", [P, WB])
        amax = tile("ff_amax", [P, WB // BLOCK])
        rs = tile("ff_rs", [P, WB // BLOCK])
        bnst = tile("ff_bn", [P, 6])
        mv = tile("ff_mv", [P, R, 2])
        sd = tile("ff_sd", [P, R])
        epst = tile("ff_eps", [P, 1])

        wg_in, wu_in, wd_in, const = sem("ff_wg"), sem("ff_wu"), sem("ff_wd"), sem("ff_const")
        zero_ok = sem("ff_zero")
        stat_ok, sd_ok, xn_ok = sem("ff_stat"), sem("ff_sdok"), sem("ff_xnok")
        chain, quant_ok = sem("ff_chain"), sem("ff_quant")
        sign_rq, sign_ok = sem("ff_sign_rq"), sem("ff_sign_ok")
        tw_ps, tw_ok = sem("ff_tw_ps"), sem("ff_tw_ok")
        gu_ps, eg_ok, gu_free = sem("ff_gu"), sem("ff_eg"), sem("ff_gufree")
        hT_ps, hT_ok, d_ps, res_ok, out_ok = (sem(n) for n in ("ff_hTps", "ff_hTok", "ff_dps", "ff_res", "ff_out"))

        Q_IN, Q_DOWN, Q_X, Q_H = 1, 2, 3, 4
        turns = []
        for m in range(2):
            for kt in range(KT):
                for j0 in (0, 4):
                    js = range(j0, min(j0 + 4, FT))
                    turns.append((Q_IN, [(win[0:rows_of(j), m, j, kt * P:(kt + 1) * P], (j - j0) * P, rows_of(j), P)
                                         for j in js],
                                  wgT[:, m, kt, j0 * P:min(F, (j0 + 4) * P)], P))
        for j in range(FT):
            turns.append((Q_DOWN, [(wdn[:, t, j * P:j * P + rows_of(j)], t * P, P, rows_of(j)) for t in range(KT)],
                          wdT[0:rows_of(j), j, :], rows_of(j)))
        for kt in range(KT):
            turns.append((Q_X, [(xn[:, r, kt * P:(kt + 1) * P], r * P, P, P) for r in range(R)], xqT[:, kt, :], P))

        block = st.enter_context(nc.Block())

        @block.sync
        def _(sp):
            full = (F // P) * P
            for m, (w, s) in enumerate(((w_gate, wg_in), (w_up, wu_in))):
                sp.dma_start(win[:, m, 0:F // P, :], w[0:full, :].rearrange("(j p) d -> p j d", p=P)).then_inc(s, 16)
                if m == 0:
                    sp.wait_ge(zero_ok, 1)
                sp.dma_start(win[0:F - full, m, F // P, :], w[full:F, :]).then_inc(s, 16)
            sp.dma_start(wdn[:, :, :], w_down.rearrange("(t p) f -> p t f", p=P)).then_inc(wd_in, 16)
            for r in range(R):
                sp.wait_ge(res_ok, r + 1)
                sp.dma_start(out.rearrange("b (t p) d -> p (b t) d", p=P)[:, r, :], res[:, r, :]).then_inc(out_ok, 16)
            sp.wait_ge(out_ok, 16 * R)

        @block.gpsimd
        def _(pool):
            pool.memset(win[:, :, FT - 1, :], 0.0).then_inc(zero_ok, 1)
            pool.memset(epst[:, :], EPS).then_inc(const, 1)

        @block.tensor
        def _(pe):
            mm = pe.matmul
            for n, (q, parts, _, _) in enumerate(turns):
                pe.wait_ge(quant_ok, q)
                if n >= 2:
                    pe.wait_ge(tw_ok, n - 1)
                for src, at, rows, cols in parts:
                    last = pe.transpose(psX[0:cols, n % 2, at:at + rows], src, ident[0:rows, 0:rows])
                last.then_inc(tw_ps, 1)
            pe.wait_ge(tw_ok, len(turns))

            def gate_up(r):
                if r >= 1:
                    pe.wait_ge(gu_free, r)
                for m, dst in enumerate((psG, psU)):
                    for c0, c1 in ((0, 512), (512, F)):
                        for kt in range(KT):
                            last = mm(dst[:, c0:c1], xqT[:, kt, r * P:(r + 1) * P], wgT[:, m, kt, c0:c1],
                                      start=(kt == 0), stop=(kt == KT - 1))
                last.then_inc(gu_ps, 1)

            def down(r):
                pe.wait_ge(quant_ok, Q_H + r)
                for half in range(2):
                    if r >= 1:
                        pe.wait_ge(hT_ok, 2 * (r - 1) + half + 1)
                    for j in range(3 * half, 3 * half + 3):
                        last = pe.transpose(psX[0:rows_of(j), half, (j % 3) * P:(j % 3 + 1) * P],
                                            hh[:, r % 2, j * P:j * P + rows_of(j)], ident[:, :])
                    last.then_inc(hT_ps, 1)
                pe.wait_ge(hT_ok, 2 * r + 2)
                if r >= 2:
                    pe.wait_ge(res_ok, r - 1)
                for j in range(FT):
                    last = mm(psD[:, r % 2, 0:D], hT[0:rows_of(j), r % 2, j, :], wdT[0:rows_of(j), j, :],
                              start=(j == 0), stop=(j == FT - 1))
                last.then_inc(d_ps, 1)

            for r in range(R + 1):
                if r < R:
                    gate_up(r)
                if r >= 1:
                    down(r - 1)

        @block.scalar
        def _(act):
            def sign(src, n, width):
                act.wait_ge(sign_rq, n)
                act.activation(absx[:, 0:width], src, ACT.Sign).then_inc(sign_ok, 1)

            flat = lambda a: a.rearrange("p a b -> p (a b)")
            act.wait_ge(stat_ok, 2 * R)
            act.wait_ge(const, 1)
            act.activation(sd[:, :], mv[:, :, 1], ACT.Sqrt, bias=epst[:, 0:1]).then_inc(sd_ok, 1)
            sign(win[:, :, :, :].rearrange("p a b c -> p (a b c)"), Q_IN, WB)
            sign(flat(wdn[:, :, :]), Q_DOWN, KT * F)
            sign(flat(xn[:, :, :]), Q_X, R * D)
            for n, (_, _, dst, rows) in enumerate(turns):
                act.wait_ge(tw_ps, n + 1)
                act.activation(dst, psX[0:rows, n % 2, 0:dst.shape[1]], ACT.Copy).then_inc(tw_ok, 1)
            for r in range(R):
                act.wait_ge(gu_ps, r + 1)
                if r >= 2:
                    act.wait_ge(quant_ok, Q_H + r - 2)
                act.activation(eg[:, r % 2, :], psG[:, 0:F], ACT.Exp, scale=-1.0).then_inc(eg_ok, 1)
                sign(hh[:, r % 2, :], Q_H + r, F)
                for half in range(2):
                    act.wait_ge(hT_ps, 2 * r + half + 1)
                    if r >= 2:
                        act.wait_ge(d_ps, r - 1)
                    if half == 0:
                        act.activation(hT[:, r % 2, 0:3, :].rearrange("p a b -> p (a b)"), psX[:, 0, 0:3 * P],
                                       ACT.Copy).then_inc(hT_ok, 1)
                    else:
                        rest = rows_of(FT - 1)
                        act.activation(hT[:, r % 2, 3:5, :].rearrange("p a b -> p (a b)"), psX[:, 1, 0:2 * P],
                                       ACT.Copy)
                        act.activation(hT[0:rest, r % 2, 5, :], psX[0:rest, 1, 2 * P:3 * P], ACT.Copy)\
                           .then_inc(hT_ok, 1)

        @block.vector
        def _(dve):
            links = [0]

            def link(ins):
                links[0] += 1
                ins.then_inc(chain, 1)
                dve.wait_ge(chain, links[0])

            def quantize(src, width, n):
                nb = width // BLOCK
                blocks = lambda a: a.rearrange("p (n k) -> p n k", k=BLOCK)
                wide = lambda a: a[:, 0:nb].unsqueeze(2).to_broadcast([P, nb, BLOCK])
                a, c = absx[:, 0:width], cnt[:, 0:width]
                link(dve.tensor_reduce(amax[:, 0:nb], blocks(src), AX.X, ALU.max, apply_absolute_value=True))
                link(dve.tensor_scalar(amax[:, 0:nb], amax[:, 0:nb], 1.0 / 6.0, 1e-12, ALU.mult, ALU.max))
                link(dve.reciprocal(rs[:, 0:nb], amax[:, 0:nb]))
                link(dve.tensor_tensor(blocks(a), blocks(src), wide(rs), ALU.mult))
                link(dve.scalar_tensor_tensor(a, a, -1.0, a, ALU.mult, ALU.max))
                link(dve.tensor_scalar(c, a, 5.0, 2.0, ALU.is_gt, ALU.mult))
                link(dve.scalar_tensor_tensor(c, a, 3.5, c, ALU.is_gt, ALU.add))
                link(dve.scalar_tensor_tensor(c, a, 2.5, c, ALU.is_gt, ALU.add))
                link(dve.tensor_scalar(c, c, 2.0, None, ALU.mult))
                for mid in (1.75, 1.25, 0.75):
                    link(dve.scalar_tensor_tensor(c, a, mid, c, ALU.is_gt, ALU.add))
                dve.scalar_tensor_tensor(c, a, 0.25, c, ALU.is_gt, ALU.add).then_inc(sign_rq, 1)
                dve.wait_ge(sign_rq, n)
                dve.wait_ge(sign_ok, n)
                link(dve.scalar_tensor_tensor(c, c, 0.5, a, ALU.mult, ALU.mult))
                dve.tensor_tensor(blocks(src), blocks(c), wide(amax), ALU.mult).then_inc(quant_ok, 1)
                dve.wait_ge(quant_ok, n)

            flat = lambda a: a.rearrange("p a b -> p (a b)")
            for r in range(R):
                if r:
                    dve.wait_ge(stat_ok, 2 * r)
                dve.bn_stats(bnst[:, :], y[:, r, :]).then_inc(stat_ok, 1)
                dve.wait_ge(stat_ok, 2 * r + 1)
                dve.bn_aggr(mv[:, r, :], bnst[:, :]).then_inc(stat_ok, 1)
            dve.wait_ge(wg_in, 32)
            dve.wait_ge(wu_in, 32)
            quantize(win[:, :, :, :].rearrange("p a b c -> p (a b c)"), WB, Q_IN)
            dve.wait_ge(wd_in, 16)
            quantize(flat(wdn[:, :, :]), KT * F, Q_DOWN)
            dve.wait_ge(sd_ok, 1)
            dve.reciprocal(sd[:, :], sd[:, :]).then_inc(sd_ok, 1)
            dve.wait_ge(sd_ok, 2)
            for r in range(R):
                dve.tensor_scalar(xn[:, r, :], y[:, r, :], mv[:, r, 0:1], sd[:, r:r + 1], ALU.subtract, ALU.mult)\
                   .then_inc(xn_ok, 1)
            dve.wait_ge(xn_ok, R)
            quantize(flat(xn[:, :, :]), R * D, Q_X)

            def finish(r):
                dve.wait_ge(d_ps, r + 1)
                dve.tensor_tensor(res[:, r, :], psD[:, r % 2, 0:D], y[:, r, :], ALU.add).then_inc(res_ok, 1)

            for r in range(R):
                i = r % 2
                e = eg[:, i, :]
                dve.wait_ge(eg_ok, r + 1)
                if r >= 2:
                    dve.wait_ge(hT_ps, 2 * (r - 1))
                link(dve.tensor_scalar(e, e, 1.0, None, ALU.add))
                link(dve.reciprocal(e, e))
                link(dve.tensor_tensor(e, psG[:, 0:F], e, ALU.mult))
                dve.tensor_tensor(hh[:, i, :], psU[:, 0:F], e, ALU.mult).then_inc(gu_free, 1)
                dve.wait_ge(gu_free, r + 1)
                quantize(hh[:, i, :], F, Q_H + r)
                if r >= 1:
                    finish(r - 1)
            finish(R - 1)


def perceiver_layer(nc, x, ctx, xWq, xbq, xWk, xbk, xWv, xbv, xWo, xbo, W_q, W_k, W_v, W_o, W_down_kv, W_up_k,
                    W_up_v, w_gate, w_up, w_down, out):
    B, S, D = x.shape
    with nc.sbuf_tensor("ident", [P, P], F32) as ident, nc.sbuf_tensor("y", [P, B * S // P, D], F32) as y:
        cross_attention(nc, x, ctx, xWq, xbq, xWk, xbk, xWv, xbv, xWo, ident, y)
        self_attention(nc, W_q, W_k, W_v, W_o, W_down_kv, W_up_k, W_up_v, xbo, ident, y)
        fp4_ffn(nc, w_gate, w_up, w_down, ident, y, out)


_INS = ['x', 'ctx_1024', 'L0_xattn_Wq', 'L0_xattn_bq', 'L0_xattn_Wk', 'L0_xattn_bk', 'L0_xattn_Wv', 'L0_xattn_bv',
        'L0_xattn_Wo', 'L0_xattn_bo', 'L0_attn_W_q', 'L0_attn_W_k', 'L0_attn_W_v', 'L0_attn_W_o',
        'L0_attn_W_down_kv', 'L0_attn_W_up_k', 'L0_attn_W_up_v', 'L0_ffn_w_gate', 'L0_ffn_w_up', 'L0_ffn_w_down']


def kernel(**inputs):
    import numpy as _np
    import concourse.bacc as _bacc
    from concourse import mybir as _mybir
    from concourse.bass_utils import run_bass_kernel_spmd as _run

    nc = _bacc.Bacc("TRN2", target_bir_lowering=False, num_devices=1)
    arrays, args = {}, []
    for name in _INS:
        a = _np.ascontiguousarray(inputs[name])
        arrays[f"in_{name}_dram"] = a
        args.append(nc.dram_tensor(f"in_{name}_dram", a.shape, _mybir.dt.from_np(a.dtype), kind="ExternalInput").ap())
    shape = inputs["x"].shape
    args.append(nc.dram_tensor("out_0_dram", shape, _mybir.dt.float32, kind="ExternalOutput").ap())
    perceiver_layer(nc, *args)
    r = _run(nc, [arrays], core_ids=[0])
    return r.results[0]["out_0_dram"]
```
